# Optimizing a Trainium2 kernel written in Bass

```python
import numpy as np
import jax
import jax.numpy as jnp

def _softmax(x, axis=-1):
    return jax.nn.softmax(x, axis=axis)

def _gelu(x):
    return jax.nn.gelu(x, approximate=True)

def _silu(x):
    return jax.nn.silu(x)

def _sigmoid(x):
    return jax.nn.sigmoid(x)

def _layernorm(x, axis=-1, eps=1e-05):
    m = jnp.mean(x, axis=axis, keepdims=True)
    v = jnp.var(x, axis=axis, keepdims=True)
    return (x - m) / jnp.sqrt(v + eps)

def _scatter_add(tgt, idx, src, axis=0):
    return tgt.at[idx].add(src)

def _segment_sum(src, seg, n):
    return jax.ops.segment_sum(src, seg, n)
kernel_name = 'mk_gnn_preln_d1_gnn_r8_e49cb8'

def setup_inputs(seed: int=0):
    np.random.seed(seed)
    _w = jnp.asarray

    def _rec_inputs():
        import jax
        import jax.numpy as jnp
        _gk = jax.random.key(seed)
        x = -0.0003713 + 1 * jax.random.normal(jax.random.fold_in(_gk, 1), (6250, 256), jnp.float32)
        src = jax.random.randint(jax.random.fold_in(_gk, 2), (100000,), 0, 6250, jnp.int32)
        dst = jax.random.randint(jax.random.fold_in(_gk, 3), (100000,), 0, 6250, jnp.int32)
        _o = jnp.argsort(dst, stable=True)
        src = src[_o]
        dst = dst[_o]
        return (x, src, dst)
    x, src, dst = _rec_inputs()

    def _L0_gnn_setup():
        import jax, jax.numpy as jnp
        import numpy as np
        N = 6250
        E = 100000
        C = 256
        NOUT = 64
        NL = 4

        def _glorot(key, shape):
            fan_in, fan_out = (shape[-2], shape[-1])
            lim = np.sqrt(6.0 / (fan_in + fan_out)).astype(np.float32)
            return jax.random.uniform(key, shape, jnp.float32, -lim, lim)
        key = jax.random.key(seed)
        ks = jax.random.split(key, 16)
        inp = {'x': jax.random.normal(ks[0], (N, C), jnp.float32), 'src': jax.random.randint(ks[1], (E,), 0, N, jnp.int32), 'dst': jax.random.randint(ks[2], (E,), 0, N, jnp.int32), 'W1s': _glorot(ks[3], (NL - 1, C, C)), 'b1s': jax.random.normal(ks[4], (NL - 1, C), jnp.float32) * 0.01, 'W2s': _glorot(ks[5], (NL - 1, C, C)), 'b2s': jax.random.normal(ks[6], (NL - 1, C), jnp.float32) * 0.01, 'W3s': _glorot(ks[7], (NL - 1, C, C)), 'b3s': jax.random.normal(ks[8], (NL - 1, C), jnp.float32) * 0.01, 'cW1': _glorot(ks[9], (C, C)), 'cb1': jax.random.normal(ks[10], (C,), jnp.float32) * 0.01, 'cW2': _glorot(ks[11], (C, NOUT)), 'cb2': jax.random.normal(ks[12], (NOUT,), jnp.float32) * 0.01, 'cW3': _glorot(ks[13], (NOUT, C)), 'cb3': jax.random.normal(ks[14], (C,), jnp.float32) * 0.01}
        return inp
    _L0_gnn_all = _L0_gnn_setup()
    _L0_gnn_in = {k: v for k, v in _L0_gnn_all.items() if k in ('W1s', 'b1s', 'W2s', 'b2s', 'W3s', 'b3s', 'cW1', 'cb1', 'cW2', 'cb2', 'cW3', 'cb3')}
    del _L0_gnn_all
    return {'x': x, 'src': src, 'dst': dst, 'L0_gnn_W1s': _L0_gnn_in['W1s'], 'L0_gnn_b1s': _L0_gnn_in['b1s'], 'L0_gnn_W2s': _L0_gnn_in['W2s'], 'L0_gnn_b2s': _L0_gnn_in['b2s'], 'L0_gnn_W3s': _L0_gnn_in['W3s'], 'L0_gnn_b3s': _L0_gnn_in['b3s'], 'L0_gnn_cW1': _L0_gnn_in['cW1'], 'L0_gnn_cb1': _L0_gnn_in['cb1'], 'L0_gnn_cW2': _L0_gnn_in['cW2'], 'L0_gnn_cb2': _L0_gnn_in['cb2'], 'L0_gnn_cW3': _L0_gnn_in['cW3'], 'L0_gnn_cb3': _L0_gnn_in['cb3']}

def reference(x, src, dst, L0_gnn_W1s, L0_gnn_b1s, L0_gnn_W2s, L0_gnn_b2s, L0_gnn_W3s, L0_gnn_b3s, L0_gnn_cW1, L0_gnn_cb1, L0_gnn_cW2, L0_gnn_cb2, L0_gnn_cW3, L0_gnn_cb3):
    import jax
    import jax.numpy as jnp

    def _L0_gnn_ref(x, src, dst, W1s, b1s, W2s, b2s, W3s, b3s, cW1, cb1, cW2, cb2, cW3, cb3):
        import jax, jax.numpy as jnp
        import numpy as np
        N = 6250
        E = 100000
        C = 256
        NOUT = 64
        NL = 4

        def _glorot(key, shape):
            fan_in, fan_out = (shape[-2], shape[-1])
            lim = np.sqrt(6.0 / (fan_in + fan_out)).astype(np.float32)
            return jax.random.uniform(key, shape, jnp.float32, -lim, lim)

        def agg(h):
            return jax.ops.segment_sum(h[src], dst, num_segments=N)
        for l in range(NL - 1):
            h = x + agg(x)
            h = jax.nn.relu(h @ W1s[l] + b1s[l])
            h = jax.nn.relu(h @ W2s[l] + b2s[l])
            x = h @ W3s[l] + b3s[l]
        h = x + agg(x)
        h = jax.nn.relu(h @ cW1 + cb1)
        h = jax.nn.relu(h @ cW2 + cb2)
        return h @ cW3 + cb3
    h = jnp.maximum(_layernorm(x, axis=-1), 0.0)
    x = x + _L0_gnn_ref(h, src, dst, L0_gnn_W1s, L0_gnn_b1s, L0_gnn_W2s, L0_gnn_b2s, L0_gnn_W3s, L0_gnn_b3s, L0_gnn_cW1, L0_gnn_cb1, L0_gnn_cW2, L0_gnn_cb2, L0_gnn_cW3, L0_gnn_cb3)
    return x

_drawn_inputs = setup_inputs


def setup_inputs(seed=0):
    import zlib

    import numpy as np

    out = dict(_drawn_inputs(seed))
    spreads = {}
    factors = {'x': 36.531,
     'L0_gnn_b1s': 64.0,
     'L0_gnn_b2s': 39.015,
     'L0_gnn_b3s': 29.823,
     'L0_gnn_cb1': 200.0,
     'L0_gnn_cb2': 200.0,
     'L0_gnn_cb3': 200.0}
    for name, (base, spread) in spreads.items():
        noise = np.random.default_rng([zlib.crc32(name.encode()), seed]).standard_normal(out[name].shape)
        drawn = base * np.exp(spread * noise) if base else spread * noise
        out[name] = jnp.asarray(drawn.astype(out[name].dtype))
    for name, factor in factors.items():
        out[name] = (out[name] * factor).astype(out[name].dtype)
    return out
```

```python
from contextlib import ExitStack, contextmanager

import concourse.bass as bass
from concourse import mybir

ALU = mybir.AluOpType
ACT = mybir.ActivationFunctionType
AX = mybir.AxisListType
F32 = mybir.dt.float32
BF16 = mybir.dt.bfloat16
I32 = mybir.dt.int32
U32 = mybir.dt.uint32

P = 128
EPS = 1e-5


def gnn(nc, x, src_cols, src_tail, dst_cols, dst_tail, dst, W1s, b1s, W2s, b2s, W3s, b3s,
        cW1, cb1, cW2, cb2, cW3, cb3, out):
    N, C = x.shape
    E = dst.shape[0]
    NL = W1s.shape[0]
    MID = cW2.shape[1]
    KC = C // P
    ND = -(-N // P)
    NLAST = N - (ND - 1) * P
    NROW = ND * P
    ET = -(-E // P)
    EFULL = E // P
    ETAIL = E - EFULL * P
    RING = 16
    HALF = RING // 2
    STEPS = -(-ET // RING)
    SWEEP = STEPS * RING
    SEL = 16
    PARTS = 3
    PW = PARTS * C
    GRP = 7
    NG = ND // GRP
    EC = -(-ET // P)
    BIG = 16384.0
    assert NG * GRP == ND and C == 256 and ETAIL > 0 and EFULL + 1 == ET and MID <= P

    tables = [nc.dram_tensor(f"nodes{layer}", (NROW, PW), BF16, kind="Internal").ap() for layer in range(NL + 1)]

    with ExitStack() as ctx:
        def sb(name, shape, dt):
            return ctx.enter_context(nc.sbuf_tensor(name, shape, dt))

        def ps(name, shape):
            return ctx.enter_context(nc.psum_tensor(name, shape, F32))

        def sem(name):
            return ctx.enter_context(nc.semaphore(name))

        xin = sb("xin", [P, ND, C], F32)
        parts = sb("parts", [P, ND, PW], BF16)
        pool_words = sb("pool_words", [P, RING * PW // 2], F32)
        ring = pool_words[:, :].bitcast(BF16).rearrange("p (r c) -> p r c", r=RING)
        select = sb("select", [P, SEL * P], BF16)
        src_i = sb("src_i", [P, SWEEP], I32)
        dst_i = sb("dst_i", [P, SWEEP], I32)
        dst_f = sb("dst_f", [P, SWEEP], F32)
        staged = sb("staged", [P, RING], I32)
        dst_rows = sb("dst_rows", [P, EC, P], I32)
        tile_min = sb("tile_min", [P, EC], F32)
        tile_max = sb("tile_max", [P, EC], F32)
        tile_no = sb("tile_no", [P, EC], F32)
        tile_key = sb("tile_key", [P, 2, EC], F32)
        node_lo = sb("node_lo", [P, ND], F32)
        node_hi = sb("node_hi", [P, ND], F32)
        neg_base = sb("neg_base", [P, ND], F32)
        cand = sb("cand", [P, 2, ND, EC], F32)
        bound = sb("bound", [P, 2, ND], F32)
        bcol = sb("bcol", [ND, 2], F32)
        row = sb("row", [1, 8, ND + 1], F32)
        flag = sb("flag", [1, 8], F32)
        walk_f = sb("walk_f", [1, ND + 1, 8], F32)
        walk = sb("walk", [1, (ND + 1) * 8], I32)
        lane = sb("lane", [P, P], F32)
        lane_bf = sb("lane_bf", [P, P], BF16)
        part_no = sb("part_no", [P, 1], F32)
        ident = sb("ident", [P, P], F32)
        ident_bf = sb("ident_bf", [P, P], BF16)
        eps = sb("eps", [P, 1], F32)
        stats = sb("stats", [P, GRP, 6], F32)
        moments = sb("moments", [P, NG, GRP, 2], F32)
        std = sb("std", [P, NG, GRP], F32)
        rstd = sb("rstd", [P, NG, GRP], F32)
        z = pool_words[:, 0:2 * GRP * C].rearrange("p (b t c) -> p b t c", b=2, t=GRP)
        w1 = sb("w1", [P, NL, KC, C], F32)
        w2 = sb("w2", [P, NL, KC, C], F32)
        w3 = sb("w3", [P, NL, KC, C], F32)
        c1 = sb("c1", [P, KC, C], F32)
        c2 = sb("c2", [P, KC, MID], F32)
        c3 = sb("c3", [MID, C], F32)
        bias1 = sb("bias1", [P, (NL + 1) * KC], F32)
        bias2 = sb("bias2", [P, (NL + 1) * KC], F32)
        bias3 = sb("bias3", [P, NL + 1, C], F32)
        agg = sb("agg", [P, C], F32)
        aggT = sb("aggT", [P, KC, P], F32)
        h1 = sb("h1", [P, KC, P], F32)
        h2 = sb("h2", [P, KC, P], F32)
        y = sb("y", [P, C], F32)
        rest = sb("rest", [P, C], F32)

        ps_agg = ps("ps_agg", [P, C])
        ps_t = ps("ps_t", [P, KC, P])
        ps_1 = ps("ps_1", [P, KC, P])
        ps_2 = ps("ps_2", [P, KC, P])
        ps_3 = ps("ps_3", [P, C])
        ps_w = ps("ps_w", [P, 2, P])
        ps_r = ps("ps_r", [1, 2, P])

        cleared = sem("cleared")
        edges_in = sem("edges_in")
        x_in = [sem(f"x_in{g}") for g in range(NG)]
        const_in = sem("const_in")
        made = sem("made")
        dve_step = sem("dve_step")
        bounds_turned = sem("bounds_turned")
        walk_ready = sem("walk_ready")
        const_ready = sem("const_ready")
        var_ready = sem("var_ready")
        std_ready = sem("std_ready")
        z_ready = sem("z_ready")
        z_hi = sem("z_hi")
        z_rest = sem("z_rest")
        z_mid = sem("z_mid")
        z_done = sem("z_done")
        written = sem("written")
        stage_ready = sem("stage_ready")
        arrived = [sem(f"arrived{k}") for k in range(RING)]
        rows_here = sem("rows_here")
        rows_free = sem("rows_free")
        sel_ready = sem("sel_ready")
        sel_free = sem("sel_free")
        passed = sem("passed")
        agg_ready = sem("agg_ready")
        agg_out = sem("agg_out")
        turned = sem("turned")
        turned_out = sem("turned_out")
        mm1 = sem("mm1")
        h1_ready = sem("h1_ready")
        mm2 = sem("mm2")
        h2_ready = sem("h2_ready")
        mm3 = sem("mm3")
        y_ready = sem("y_ready")
        hi_ready = sem("hi_ready")
        rest_ready = sem("rest_ready")
        mid_ready = sem("mid_ready")
        lo_ready = sem("lo_ready")
        stored = sem("stored")

        N_EDGE_DMA = 7
        N_CONST_DMA = 4 + 2 + 3 + 3 * NL

        def totals(eng):
            sweeps = eng.value_load(walk[0:1, 8 * ND:8 * ND + 1], min_val=1, max_val=ND)
            pairs = eng.value_load(walk[0:1, 8 * ND + 1:8 * ND + 2], min_val=ET, max_val=ND * ET)
            return sweeps, pairs

        def steps_of(eng, node_tile):
            at = node_tile * 8

            def load(k, least, most):
                return eng.value_load(walk[0:1, bass.ds(at + k, 1)], min_val=least, max_val=most)
            return (load(0, 0, ET - 1), load(1, 1, ET), load(2, 0, ND * SWEEP), load(3, 0, ND * ET))

        block = ctx.enter_context(nc.Block())

        @block.sync
        def _(sp):
            sp.wait_ge(cleared, 4)
            sp.dma_start(dst_rows[:, 0:EC - 1, :], dst[0:(EC - 1) * P * P].rearrange(
                "(c p e) -> p c e", p=P, e=P)).then_inc(edges_in, 16)
            left = EFULL - (EC - 1) * P
            sp.dma_start(dst_rows[0:left, EC - 1, :], dst[(EC - 1) * P * P:EFULL * P].rearrange(
                "(p e) -> p e", e=P)).then_inc(edges_in, 16)
            sp.dma_start(dst_rows[left:left + 1, EC - 1, 0:ETAIL],
                         dst[EFULL * P:E].rearrange("(a e) -> a e", a=1)).then_inc(edges_in, 16)
            sp.dma_start(src_i[:, 0:EFULL], src_cols).then_inc(edges_in, 16)
            sp.dma_start(src_i[0:ETAIL, EFULL:ET], src_tail).then_inc(edges_in, 16)
            sp.dma_start(dst_i[:, 0:EFULL], dst_cols).then_inc(edges_in, 16)
            sp.dma_start(dst_i[0:ETAIL, EFULL:ET], dst_tail).then_inc(edges_in, 16)
            with nc.allow_non_contiguous_dma(reason="biases by channel, once"):
                for b, (hidden, last) in ((bias1, (b1s, cb1)), (bias2, (b2s, None))):
                    sp.dma_start(b[:, 0:NL * KC], hidden.rearrange("l (k p) -> p (l k)", p=P)).then_inc(const_in, 16)
                    if last is not None:
                        sp.dma_start(b[:, NL * KC:], last.rearrange("(k p) -> p k", p=P)).then_inc(const_in, 16)
                sp.dma_start(bias2[0:MID, NL * KC:NL * KC + 1], cb2.rearrange("(p a) -> p a", a=1)).then_inc(const_in, 16)
            sp.dma_start(bias3[:, 0:NL, :], b3s.partition_broadcast(P)).then_inc(const_in, 16)
            sp.dma_start(bias3[:, NL, :], cb3.partition_broadcast(P)).then_inc(const_in, 16)
            sp.dma_start(c1[:, :, :], cW1.rearrange("(k p) m -> p k m", p=P)).then_inc(const_in, 16)
            sp.dma_start(c2[:, :, :], cW2.rearrange("(k p) m -> p k m", p=P)).then_inc(const_in, 16)
            sp.dma_start(c3[:, :], cW3).then_inc(const_in, 16)

            for w, source in ((w1, W1s), (w2, W2s), (w3, W3s)):
                for layer in range(NL):
                    sp.dma_start(w[:, layer, :, :], source[layer].rearrange("(k p) m -> p k m", p=P)
                                 ).then_inc(const_in, 16)

            sp.wait_ge(walk_ready, 1)
            sweeps, _ = totals(sp)

            def layer_rows(layer, last):
                with sp.Fori(0, sweeps * STEPS) as step:
                    rounds = (step + layer * (sweeps * STEPS) + 1) * 16
                    for k in range(RING):
                        sp.wait_ge(arrived[k], rounds)
                        sp.sem_inc(rows_here, 1)

            for layer in range(NL + 1):
                layer_rows(layer, layer == NL)
            sp.wait_ge(written, 16 * (NG + NL * ND))
            sp.wait_ge(stored, 16 * ND)

        @block.gpsimd
        def _(pool):
            pool.iota(lane[:, :], pattern=[[1, P]], base=0, channel_multiplier=0,
                      allow_small_or_imprecise_dtypes=True).then_inc(made, 1)
            pool.iota(part_no[:, :], pattern=[[1, 1]], base=0, channel_multiplier=1,
                      allow_small_or_imprecise_dtypes=True).then_inc(made, 1)
            pool.iota(tile_no[:, :], pattern=[[P, EC]], base=0, channel_multiplier=1,
                      allow_small_or_imprecise_dtypes=True).then_inc(made, 1)
            pool.iota(node_lo[:, :], pattern=[[P, ND]], base=0, channel_multiplier=0,
                      allow_small_or_imprecise_dtypes=True).then_inc(made, 1)
            pool.iota(node_hi[:, :], pattern=[[P, ND]], base=P - 1, channel_multiplier=0,
                      allow_small_or_imprecise_dtypes=True).then_inc(made, 1)
            pool.iota(row[0:1, 7, :], pattern=[[1, ND + 1]], base=0, channel_multiplier=0,
                      allow_small_or_imprecise_dtypes=True).then_inc(made, 1)
            pool.wait_ge(walk_ready, 1)
            sweeps, _ = totals(pool)
            pool.wait_ge(edges_in, 16 * N_EDGE_DMA)

            def layer_gathers(layer, last):
                pool.wait_ge(written, (NG + layer * ND) * 16)
                pool.sem_inc(passed, 1)
                with pool.Fori(0, sweeps) as sweep:
                    with pool.Fori(0, STEPS) as step:
                        rounds = pool.snap(step + (sweep + layer * sweeps) * STEPS)
                        for k in range(RING):
                            if k % HALF == 0:
                                half = k // HALF
                                pool.wait_ge(rows_free, rounds * RING + (k + HALF))
                                pool.sem_inc(passed, 1)
                                pool.tensor_copy(staged[:, k:k + HALF], src_i[:, bass.ds(step * RING + k, HALF)]
                                                 ).then_inc(stage_ready, 1)
                                pool.wait_ge(stage_ready, rounds * 2 + (half + 1))
                                pool.sem_inc(passed, 1)
                            pool.indirect_dma_start(
                                ring[:, k, :], None, tables[layer],
                                bass.IndirectOffsetOnAxis(ap=staged[:, k:k + 1].bitcast(U32), axis=0),
                            ).then_inc(arrived[k], 16)

            for layer in range(NL + 1):
                layer_gathers(layer, layer == NL)

        @block.vector
        def _(dve):
            dve.memset(dst_rows[:, :, :], int(BIG)).then_inc(cleared, 1)
            dve.memset(src_i[:, EFULL:], 0).then_inc(cleared, 1)
            dve.memset(dst_i[:, EFULL:], -1).then_inc(cleared, 1)
            dve.memset(xin[96:P, ND - 1, :], 0.0).then_inc(cleared, 1)
            dve.memset(eps[:, :], EPS).then_inc(const_ready, 1)

            steps = [0]

            def step(instruction):
                steps[0] += 1
                instruction.then_inc(dve_step, 1)
                dve.wait_ge(dve_step, steps[0])

            dve.wait_ge(made, 6)
            dve.tensor_scalar(ident[:, :], lane[:, :], part_no[:, 0:1], None, ALU.is_equal).then_inc(const_ready, 1)
            dve.tensor_scalar(ident_bf[:, :], lane[:, :], part_no[:, 0:1], None, ALU.is_equal).then_inc(const_ready, 1)
            dve.tensor_copy(lane_bf[:, :], lane[:, :]).then_inc(const_ready, 1)
            dve.tensor_scalar(neg_base[:, :], node_lo[:, :], -1.0, None, ALU.mult).then_inc(const_ready, 1)

            def normalise(g):
                dve.wait_ge(std_ready, g + 1)
                step(dve.reciprocal(rstd[:, g, :], std[:, g, :]))
                if g >= 2:
                    dve.wait_ge(z_done, g - 1)
                for t in range(GRP):
                    last = dve.tensor_scalar(z[:, g % 2, t, :], xin[:, g * GRP + t, :], moments[:, g, t, 0:1],
                                             rstd[:, g, t:t + 1], ALU.subtract, ALU.mult)
                last.then_inc(z_ready, 1)

            def group(g):
                return parts[:, g * GRP:(g + 1) * GRP, :]

            def split(g):
                dve.wait_ge(z_hi, g + 1)
                dve.wait_ge(z_ready, g + 1)
                dve.scalar_tensor_tensor(out=z[:, g % 2, :, :], in0=z[:, g % 2, :, :], scalar=0.0,
                                         in1=group(g)[:, :, 0:C], op0=ALU.max, op1=ALU.subtract).then_inc(z_rest, 1)
                dve.wait_ge(z_mid, g + 1)
                dve.wait_ge(z_rest, g + 1)
                dve.tensor_tensor(group(g)[:, :, 2 * C:], z[:, g % 2, :, :], group(g)[:, :, C:2 * C],
                                  ALU.subtract).then_inc(z_done, 1)

            def moments_step(g):
                dve.wait_ge(x_in[g], 16 if g < NG - 1 else 32)
                for t in range(GRP):
                    last = dve.bn_stats(stats[:, t, :], xin[:, g * GRP + t, :])
                step(last)
                for t in range(GRP):
                    last = dve.bn_aggr(moments[:, g, t, :], stats[:, t, :])
                last.then_inc(var_ready, 1)

            moments_step(0)
            normalise(0)
            for g in range(NG):
                if g + 1 < NG:
                    moments_step(g + 1)
                    normalise(g + 1)
                split(g)

            dve.wait_ge(edges_in, 16 * N_EDGE_DMA)
            dve.tensor_reduce(tile_min[:, :], dst_rows[:, :, :], AX.X, ALU.min)
            step(dve.tensor_reduce(tile_max[:, :], dst_rows[:, :, :], AX.X, ALU.max))
            dve.tensor_scalar(tile_key[:, 0, :], tile_no[:, :], -BIG, None, ALU.add)
            step(dve.tensor_scalar(tile_key[:, 1, :], tile_no[:, :], 1.0, None, ALU.add))
            for c in range(EC):
                dve.tensor_scalar(cand[:, 0, :, c], node_lo[:, :], tile_max[:, c:c + 1], tile_key[:, 0, c:c + 1],
                                  ALU.is_le, ALU.mult)
                last = dve.tensor_scalar(cand[:, 1, :, c], node_hi[:, :], tile_min[:, c:c + 1],
                                         tile_key[:, 1, c:c + 1], ALU.is_ge, ALU.mult)
            step(last)
            dve.tensor_reduce(bound[:, 0, :], cand[:, 0, :, :], AX.X, ALU.min)
            step(dve.tensor_reduce(bound[:, 1, :], cand[:, 1, :, :], AX.X, ALU.max))
            dve.sem_inc(bounds_turned, 1)
            dve.wait_ge(bounds_turned, 2)
            dve.tensor_reduce(bcol[:, 0:1], ps_w[0:ND, 0, :], AX.X, ALU.min)
            dve.tensor_reduce(bcol[:, 1:2], ps_w[0:ND, 1, :], AX.X, ALU.max).then_inc(bounds_turned, 1)
            dve.wait_ge(bounds_turned, 4)
            dve.tensor_scalar(row[:, 0, 0:ND], ps_r[:, 0, 0:ND], BIG, None, ALU.add)
            dve.tensor_copy(row[:, 1, 0:ND], ps_r[:, 1, 0:ND])
            step(dve.memset(row[:, 2, ND - 1:ND], float(ET - 1)))
            step(dve.tensor_copy(row[:, 2, 0:ND - 1], row[:, 0, 1:ND]))
            step(dve.tensor_tensor(row[:, 3, 0:ND], row[:, 1, 0:ND], row[:, 2, 0:ND], ALU.subtract))
            step(dve.tensor_reduce(flag[:, 0:1], row[:, 3, 0:ND], AX.X, ALU.max))
            step(dve.tensor_scalar(flag[:, 1:2], flag[:, 0:1], 1.5, None, ALU.is_ge))
            dve.tensor_scalar(flag[:, 2:3], flag[:, 1:2], -1.0, 1.0, ALU.mult, ALU.add)
            dve.tensor_scalar(flag[:, 3:4], flag[:, 1:2], float(SWEEP), None, ALU.mult)
            step(dve.tensor_scalar(flag[:, 4:5], flag[:, 1:2], float(ET - 1), 1.0, ALU.mult, ALU.add))
            step(dve.memset(walk_f[:, :, :], 0.0))
            dve.tensor_scalar(walk_f[:, 0:ND, 0], row[:, 0, 0:ND], flag[:, 2:3], None, ALU.mult)
            step(dve.tensor_scalar(row[:, 4, 0:ND], row[:, 2, 0:ND], float(-(ET - 1)), None, ALU.add))
            dve.tensor_scalar(walk_f[:, 0:ND, 1], row[:, 4, 0:ND], flag[:, 2:3], float(ET), ALU.mult, ALU.add)
            dve.tensor_scalar(walk_f[:, 0:ND, 2], row[:, 7, 0:ND], flag[:, 3:4], None, ALU.mult)
            dve.tensor_scalar(walk_f[:, 0:ND, 3], row[:, 7, 0:ND], flag[:, 4:5], None, ALU.mult)
            dve.tensor_scalar(walk_f[:, 0:ND, 4], row[:, 7, 0:ND], float(ND - 1), flag[:, 1:2], ALU.is_ge, ALU.max)
            dve.tensor_scalar(walk_f[:, ND, 0:1], flag[:, 1:2], float(ND - 1), 1.0, ALU.mult, ALU.add)
            step(dve.tensor_scalar(walk_f[:, ND, 1:2], flag[:, 1:2], float(ND * ET - (ET + ND - 1)),
                                   float(ET + ND - 1), ALU.mult, ALU.add))
            dve.tensor_copy(walk[:, :], walk_f[:, :, :].rearrange("a b c -> a (b c)")).then_inc(walk_ready, 1)
            step(dve.tensor_copy(dst_f[:, :], dst_i[:, :]))
            dve.wait_ge(const_ready, 5)
            dve.wait_ge(walk_ready, 1)
            _, pairs = totals(dve)
            dve.wait_ge(const_in, 16 * N_CONST_DMA)

            def layer_sums(layer, last):
                before = dve.snap(layer * pairs)
                with dve.Fori(0, ND) as d:
                    n = dve.snap(layer * ND + d)
                    first, end, _, pair0 = steps_of(dve, d)
                    shift = dve.snap(pair0 + before)
                    with dve.Fori(first, end) as t:
                        pair = dve.snap(t + shift)
                        dve.wait_ge(sel_free, pair + 1)
                        dve.tensor_scalar(select[:, bass.ds((pair & (SEL - 1)) * P, P)], lane[:, :],
                                          dst_f[:, bass.ds(t, 1)], neg_base[:, bass.ds(d, 1)],
                                          ALU.subtract, ALU.is_equal).then_inc(sel_ready, 1)
                    dve.wait_ge(turned, n + 1)
                    dve.tensor_copy(aggT[:, :, :], ps_t[:, :, :]).then_inc(turned_out, 1)
                    dve.wait_ge(mm3, n + 1)
                    dve.tensor_tensor(y[:, :], ps_3[:, :], bias3[:, layer, :], ALU.add).then_inc(y_ready, 1)
                    dve.wait_ge(y_ready, n + 1)
                    here = xin if last else parts
                    tile = here[:, bass.ds(d, 1), :].rearrange("p a c -> p (a c)")
                    if last:
                        dve.tensor_tensor(tile, tile, y[:, :], ALU.add).then_inc(lo_ready, 1)
                    else:
                        dve.wait_ge(hi_ready, n + 1)
                        dve.tensor_tensor(rest[:, :], y[:, :], tile[:, 0:C], ALU.subtract).then_inc(rest_ready, 1)
                        dve.wait_ge(mid_ready, n + 1)
                        dve.tensor_tensor(tile[:, 2 * C:3 * C], rest[:, :], tile[:, C:2 * C],
                                          ALU.subtract).then_inc(lo_ready, 1)

            for layer in range(NL + 1):
                layer_sums(layer, layer == NL)

        @block.scalar
        def _(act):
            act.wait_ge(cleared, 4)
            for g in range(NG):
                tiles = GRP if g < NG - 1 else GRP - 1
                act.dma_start(xin[:, g * GRP:g * GRP + tiles, :],
                              x[g * GRP * P:(g * GRP + tiles) * P, :].rearrange("(t p) c -> p t c", p=P)
                              ).then_inc(x_in[g], 16)
            act.dma_start(xin[0:NLAST, ND - 1, :], x[(ND - 1) * P:N, :]).then_inc(x_in[NG - 1], 16)
            act.wait_ge(const_ready, 1)

            def root(g):
                act.wait_ge(var_ready, g + 1)
                act.activation(std[:, g, :], moments[:, g, :, 1], ACT.Sqrt, bias=eps[:, 0:1]).then_inc(std_ready, 1)

            def split(g):
                mine = parts[:, g * GRP:(g + 1) * GRP, :]
                act.wait_ge(z_ready, g + 1)
                act.activation(mine[:, :, 0:C], z[:, g % 2, :, :], ACT.Relu).then_inc(z_hi, 1)
                act.wait_ge(z_rest, g + 1)
                act.copy(mine[:, :, C:2 * C], z[:, g % 2, :, :]).then_inc(z_mid, 1)
                act.wait_ge(z_done, g + 1)
                act.dma_start(tables[0][g * GRP * P:(g + 1) * GRP * P, :].rearrange("(t p) c -> p t c", p=P),
                              mine).then_inc(written, 16)

            root(0)
            for g in range(NG):
                if g + 1 < NG:
                    root(g + 1)
                split(g)
            act.wait_ge(walk_ready, 1)
            sweeps, _ = totals(act)
            act.wait_ge(const_in, 16 * N_CONST_DMA)

            def layer_mlp(layer, last):
                def node_tile(d, nodes):
                    n = act.snap(layer * ND + d)
                    act.wait_ge(agg_ready, n + 1)
                    act.copy(agg[:, :], ps_agg[:, :]).then_inc(agg_out, 1)
                    ends = act.value_load(walk[0:1, bass.ds(d * 8 + 4, 1)], min_val=0, max_val=1)
                    row0 = act.value_load(walk[0:1, bass.ds(d * 8 + 2, 1)], min_val=0, max_val=ND * SWEEP)
                    with act.If(ends > 0):
                        act.wait_ge(rows_here, row0 + (layer * (sweeps * SWEEP) + SWEEP))
                        act.sem_inc(rows_free, SWEEP - ET + 1)
                    rows1, rows2 = (P, MID) if last else (P, P)
                    for ready, held, hidden, bias, done, rows in (
                            (mm1, ps_1, h1, bias1, h1_ready, P), (mm2, ps_2, h2, bias2, h2_ready, rows2)):
                        act.wait_ge(ready, n + 1)
                        for k in range(KC if rows == P else 1):
                            act.activation(hidden[0:rows, k, :], held[0:rows, k, :], ACT.Relu,
                                           bias=bias[0:rows, layer * KC + k:layer * KC + k + 1]).then_inc(done, 1)
                    if last:
                        act.wait_ge(lo_ready, n + 1)
                        act.dma_start(out[bass.ds(d * P, nodes), :],
                                      xin[0:nodes, bass.ds(d, 1), :].rearrange("p a c -> p (a c)")
                                      ).then_inc(stored, 16)
                        return
                    mine = parts[:, bass.ds(d, 1), :].rearrange("p a c -> p (a c)")
                    act.wait_ge(y_ready, n + 1)
                    act.copy(mine[:, 0:C], y[:, :]).then_inc(hi_ready, 1)
                    act.wait_ge(rest_ready, n + 1)
                    act.copy(mine[:, C:2 * C], rest[:, :]).then_inc(mid_ready, 1)
                    act.wait_ge(lo_ready, n + 1)
                    act.dma_start(tables[layer + 1][bass.ds(d * P, P), :], mine).then_inc(written, 16)

                if last:
                    with act.Fori(0, ND - 1) as d:
                        node_tile(d, P)
                    node_tile(ND - 1, NLAST)
                else:
                    with act.Fori(0, ND) as d:
                        node_tile(d, P)

            for layer in range(NL + 1):
                layer_mlp(layer, layer == NL)

        @block.tensor
        def _(pe):
            pe.sem_inc(rows_free, RING)
            pe.sem_inc(sel_free, SEL)
            pe.wait_ge(const_ready, 5)
            pe.wait_ge(bounds_turned, 1)
            pe.transpose(ps_w[0:ND, 0, :], bound[:, 0, :], ident[:, :])
            pe.transpose(ps_w[0:ND, 1, :], bound[:, 1, :], ident[:, :]).then_inc(bounds_turned, 1)
            pe.wait_ge(bounds_turned, 3)
            pe.matmul(ps_r[:, 0, 0:ND], bcol[:, 0:1], ident[0:ND, 0:ND], start=True, stop=True)
            pe.matmul(ps_r[:, 1, 0:ND], bcol[:, 1:2], ident[0:ND, 0:ND], start=True, stop=True
                      ).then_inc(bounds_turned, 1)
            pe.wait_ge(walk_ready, 1)
            sweeps, pairs = totals(pe)
            pe.wait_ge(const_in, 16 * N_CONST_DMA)

            def layer_products(layer, last):
                pe.wait_ge(written, (NG + layer * ND) * 16)
                pe.sem_inc(passed, 1)
                before = pe.snap(layer * pairs)
                gathered = pe.snap(layer * sweeps * SWEEP)
                with pe.Fori(0, ND) as d:
                    n = pe.snap(layer * ND + d)
                    first, end, row0, pair0 = steps_of(pe, d)
                    shift = pe.snap(pair0 + before)
                    row_shift = pe.snap(row0 + gathered)

                    def own(part, **flags):
                        return pe.matmul(ps_agg[:, :], ident_bf[:, :], parts[:, bass.ds(d, 1), part * C:(part + 1) * C]
                                         .rearrange("p a c -> p (a c)"), **flags)

                    def pair(t, frees):
                        number = pe.snap(t + shift)
                        pe.wait_ge(sel_ready, number + 1)
                        pe.wait_ge(rows_here, t + row_shift + 1)
                        pe.sem_inc(passed, 1)
                        sel = select[:, bass.ds((number & (SEL - 1)) * P, P)]
                        slot = pe.snap(t & (RING - 1))
                        for part in range(PARTS):
                            mm = pe.matmul(ps_agg[:, :], sel, ring[:, bass.ds(slot, 1), part * C:(part + 1) * C]
                                           .rearrange("p a c -> p (a c)"), start=False, stop=False)
                            if part == 0 and frees:
                                mm.then_inc(rows_free, 1)
                        mm.then_inc(sel_free, 1)

                    own(0, start=True, stop=False)
                    pair(first, False)
                    with pe.If(end > first + 1):
                        with pe.Fori(first + 1, end) as t:
                            pair(t, True)
                    own(1, start=False, stop=False)
                    own(2, start=False, stop=True).then_inc(agg_ready, 1)

                    a, b, c = (c1, c2, c3) if last else (w1[:, layer], w2[:, layer], w3[:, layer])
                    pe.wait_ge(agg_out, n + 1)
                    for k in range(KC):
                        mm = pe.transpose(ps_t[:, k, :], agg[:, k * P:(k + 1) * P], ident[:, :])
                    mm.then_inc(turned, 1)
                    pe.wait_ge(turned_out, n + 1)
                    for m in range(KC):
                        for k in range(KC):
                            mm = pe.matmul(ps_1[:, m, :], a[:, k, m * P:(m + 1) * P], aggT[:, k, :],
                                           start=(k == 0), stop=(k == KC - 1))
                    mm.then_inc(mm1, 1)
                    pe.wait_ge(h1_ready, (n + 1) * KC)
                    for m in range(1 if last else KC):
                        rows = MID if last else P
                        for k in range(KC):
                            mm = pe.matmul(ps_2[0:rows, m, :], b[:, k, m * P:m * P + rows], h1[:, k, :],
                                           start=(k == 0), stop=(k == KC - 1))
                    mm.then_inc(mm2, 1)
                    if last:
                        pe.wait_ge(h2_ready, NL * ND * KC + (d + 1))
                        mm = pe.matmul(ps_3[:, :], h2[0:MID, 0, :], c[:, :], start=True, stop=True)
                    else:
                        pe.wait_ge(h2_ready, (n + 1) * KC)
                        for k in range(KC):
                            mm = pe.matmul(ps_3[:, :], h2[:, k, :], c[:, k, :], start=(k == 0), stop=(k == KC - 1))
                    mm.then_inc(mm3, 1)

            for layer in range(NL + 1):
                layer_products(layer, layer == NL)


_INS = ["x", "src", "dst", "W1s", "b1s", "W2s", "b2s", "W3s", "b3s", "cW1", "cb1", "cW2", "cb2", "cW3", "cb3"]


def kernel(**inputs):
    import numpy as np
    import concourse.bacc as bacc
    from concourse.bass_utils import run_bass_kernel_spmd

    nc = bacc.Bacc("TRN2", target_bir_lowering=False, num_devices=1)
    given = {n: np.ascontiguousarray(inputs[n if n in inputs else f"L0_gnn_{n}"]) for n in _INS}
    whole = given["src"].shape[0] // P * P

    def columns(a):
        return np.ascontiguousarray(a[:whole].reshape(-1, P).T), np.ascontiguousarray(a[whole:].reshape(-1, 1))

    arrays = {"x": given["x"]}
    arrays["src_cols"], arrays["src_tail"] = columns(given["src"])
    arrays["dst_cols"], arrays["dst_tail"] = columns(given["dst"])
    for n in _INS[2:]:
        arrays[n] = given[n]
    arrays = {f"in_{n}": a for n, a in arrays.items()}
    args = [nc.dram_tensor(n, a.shape, mybir.dt.from_np(a.dtype), kind="ExternalInput").ap() for n, a in arrays.items()]
    args.append(nc.dram_tensor("out_0", given["x"].shape, F32, kind="ExternalOutput").ap())
    gnn(nc, *args)
    return run_bass_kernel_spmd(nc, [arrays], core_ids=[0]).results[0]["out_0"]
```
